# Optimizing a Trainium2 kernel written in Bass

```python
import numpy as np
import jax
import jax.numpy as jnp

def _softmax(x, axis=-1):
    return jax.nn.softmax(x, axis=axis)
def _gelu(x):
    return jax.nn.gelu(x, approximate=True)
def _silu(x):
    return jax.nn.silu(x)
def _sigmoid(x):
    return jax.nn.sigmoid(x)
def _layernorm(x, axis=-1, eps=1e-5):
    m = jnp.mean(x, axis=axis, keepdims=True)
    v = jnp.var(x, axis=axis, keepdims=True)
    return (x - m) / jnp.sqrt(v + eps)
def _scatter_add(tgt, idx, src, axis=0):
    return tgt.at[idx].add(src)
def _segment_sum(src, seg, n):
    return jax.ops.segment_sum(src, seg, n)

kernel_name = 'mk_conv_preact_d1_conv_nhwc256_65b4f3'

def setup_inputs(seed: int = 0):
    np.random.seed(seed)
    _w = jnp.asarray
    def _rec_inputs():
        import jax
        import jax.numpy as jnp
        _gk = jax.random.key(seed)
        x = -0.000125 + 0.9999 * jax.random.normal(jax.random.fold_in(_gk, 1), (2, 256, 256, 256), jnp.float32)
        return x
    x = _rec_inputs()
    def _L0_conv_setup():
        import jax, jax.numpy as jnp
        import numpy as np
        import math
        K = 3
        PAD = 1
        S = 2
        HEADS = 8

        def _unfold(z, k, pad, s):
            B, C, H, W = z.shape
            zp = jnp.pad(z, ((0, 0), (0, 0), (pad, pad), (pad, pad)))
            oh = (H + 2 * pad - k) // s + 1
            ow = (W + 2 * pad - k) // s + 1
            ri = jnp.arange(oh)[:, None] * s + jnp.arange(k)[None, :]
            rj = jnp.arange(ow)[:, None] * s + jnp.arange(k)[None, :]
            p = zp[:, :, ri, :]
            p = p[:, :, :, :, rj]
            cols = jnp.transpose(p, (0, 1, 3, 5, 2, 4)).reshape(B, C * k * k, oh * ow)
            return cols

        def _fold(cols, out_size, k, pad, s):
            B, Ckk, L = cols.shape
            C = Ckk // (k * k)
            Ho, Wo = out_size
            oh = (Ho + 2 * pad - k) // s + 1
            ow = (Wo + 2 * pad - k) // s + 1
            patches = cols.reshape(B, C, k, k, oh, ow)
            zp = jnp.zeros((B, C, Ho + 2 * pad, Wo + 2 * pad), cols.dtype)
            for ki in range(k):
                for kj in range(k):
                    zp = zp.at[:, :, ki:ki + oh * s:s, kj:kj + ow * s:s].add(patches[:, :, ki, kj])
            return zp[:, :, pad:pad + Ho, pad:pad + Wo]
        key = jax.random.key(seed)
        k1, k2, k3, k4 = jax.random.split(key, 4)
        B, H, W, C = (2, 256, 256, 256)
        kk = K * K
        x = jax.random.normal(k1, (B, H, W, C), dtype=jnp.float32)
        attn_w = jax.random.normal(k2, (K ** 4 * HEADS, C), dtype=jnp.float32) * 0.02
        attn_b = jnp.zeros((K ** 4 * HEADS,), dtype=jnp.float32)
        fan_out = kk * C
        conv_w = jax.random.normal(k3, (kk * C, C), dtype=jnp.float32) * math.sqrt(2.0 / fan_out)
        proj_w = jax.random.normal(k4, (C, C), dtype=jnp.float32) * 0.02
        proj_b = jnp.zeros((C,), dtype=jnp.float32)
        return {'x': x, 'attn_w': attn_w, 'attn_b': attn_b, 'conv_w': conv_w, 'proj_w': proj_w, 'proj_b': proj_b}
    _L0_conv_all = _L0_conv_setup()
    _L0_conv_in = {k: v for k, v in _L0_conv_all.items() if k in ('attn_w', 'attn_b', 'conv_w', 'proj_w', 'proj_b', )}
    del _L0_conv_all

    return {
        "x": x,
        "L0_conv_attn_w": _L0_conv_in["attn_w"],
        "L0_conv_attn_b": _L0_conv_in["attn_b"],
        "L0_conv_conv_w": _L0_conv_in["conv_w"],
        "L0_conv_proj_w": _L0_conv_in["proj_w"],
        "L0_conv_proj_b": _L0_conv_in["proj_b"],
    }

def reference(x, L0_conv_attn_w, L0_conv_attn_b, L0_conv_conv_w, L0_conv_proj_w, L0_conv_proj_b):
    import jax
    import jax.numpy as jnp
    def _L0_conv_ref(x, attn_w, attn_b, conv_w, proj_w, proj_b):
        import jax, jax.numpy as jnp
        import numpy as np
        import math
        K = 3
        PAD = 1
        S = 2
        HEADS = 8

        def _unfold(z, k, pad, s):
            B, C, H, W = z.shape
            zp = jnp.pad(z, ((0, 0), (0, 0), (pad, pad), (pad, pad)))
            oh = (H + 2 * pad - k) // s + 1
            ow = (W + 2 * pad - k) // s + 1
            ri = jnp.arange(oh)[:, None] * s + jnp.arange(k)[None, :]
            rj = jnp.arange(ow)[:, None] * s + jnp.arange(k)[None, :]
            p = zp[:, :, ri, :]
            p = p[:, :, :, :, rj]
            cols = jnp.transpose(p, (0, 1, 3, 5, 2, 4)).reshape(B, C * k * k, oh * ow)
            return cols

        def _fold(cols, out_size, k, pad, s):
            B, Ckk, L = cols.shape
            C = Ckk // (k * k)
            Ho, Wo = out_size
            oh = (Ho + 2 * pad - k) // s + 1
            ow = (Wo + 2 * pad - k) // s + 1
            patches = cols.reshape(B, C, k, k, oh, ow)
            zp = jnp.zeros((B, C, Ho + 2 * pad, Wo + 2 * pad), cols.dtype)
            for ki in range(k):
                for kj in range(k):
                    zp = zp.at[:, :, ki:ki + oh * s:s, kj:kj + ow * s:s].add(patches[:, :, ki, kj])
            return zp[:, :, pad:pad + Ho, pad:pad + Wo]
        B, H, W, C = x.shape
        k, s, pad, heads = (K, S, PAD, HEADS)
        kk = k * k
        out_dim = C
        hd = out_dim // heads
        scale = hd ** (-0.5)
        h, w = (math.ceil(H / s), math.ceil(W / s))
        xb = jnp.transpose(x, (0, 3, 1, 2))
        pooled = xb.reshape(B, C, h, s, w, s).mean(axis=(3, 5))
        a = jnp.transpose(pooled, (0, 2, 3, 1)).reshape(B, h * w, C)
        a = a @ attn_w.T + attn_b
        a = a.reshape(B, h * w, heads, kk, kk).transpose(0, 2, 1, 3, 4) * scale
        a = jax.nn.softmax(a, axis=-1)
        v_in = jnp.transpose(x, (0, 2, 3, 1))
        cols = _unfold(v_in, k, pad, s)
        v = cols.reshape(B, out_dim, kk, h * w)
        v = jnp.transpose(v, (0, 3, 2, 1))
        Wp = conv_w.reshape(kk, out_dim, out_dim)
        v = jnp.einsum('blpi,poi->blpo', v, Wp)
        v = v.reshape(B, h * w, kk, heads, hd).transpose(0, 3, 1, 2, 4)
        o = jnp.einsum('bnlpq,bnlqd->bnlpd', a, v)
        o = jnp.transpose(o, (0, 1, 4, 3, 2))
        o = o.reshape(B, out_dim * kk, h * w)
        y = _fold(o, (H, W), k, pad, s)
        y = jnp.transpose(y, (0, 2, 3, 1))
        y = y @ proj_w.T + proj_b
        return y

    def _gn(v, G=32, eps=1e-5):
        B_, H_, W_, C_ = v.shape
        g = v.reshape(B_, H_, W_, G, C_ // G)
        m = jnp.mean(g, axis=(1, 2, 4), keepdims=True)
        s = jnp.var(g, axis=(1, 2, 4), keepdims=True)
        return ((g - m) / jnp.sqrt(s + eps)).reshape(v.shape)

    def _ln_c(v, eps=1e-6):
        m = jnp.mean(v, axis=-1, keepdims=True)
        s = jnp.var(v, axis=-1, keepdims=True)
        return (v - m) / jnp.sqrt(s + eps)

    def _ln_t(v, eps=1e-5):
        m = jnp.mean(v, axis=-1, keepdims=True)
        s = jnp.var(v, axis=-1, keepdims=True)
        return (v - m) / jnp.sqrt(s + eps)

    def _to_tokens(v):
        B_, H_, W_, C_ = v.shape
        return v.reshape(B_, H_ * W_, C_)
    def _from_tokens(t, like):
        return t.reshape(like.shape)

    x = x + _L0_conv_ref(_gn(x), L0_conv_attn_w, L0_conv_attn_b, L0_conv_conv_w, L0_conv_proj_w, L0_conv_proj_b)
    return x


_drawn_inputs = setup_inputs


def setup_inputs(seed=0):
    import zlib

    import numpy as np

    out = dict(_drawn_inputs(seed))
    spreads = {'L0_conv_attn_b': (0.0, 2.0), 'L0_conv_proj_b': (0.0, 0.1)}
    factors = {'L0_conv_attn_w': 28.246}
    for name, (base, spread) in spreads.items():
        noise = np.random.default_rng([zlib.crc32(name.encode()), seed]).standard_normal(out[name].shape)
        drawn = base * np.exp(spread * noise) if base else spread * noise
        out[name] = jnp.asarray(drawn.astype(out[name].dtype))
    for name, factor in factors.items():
        out[name] = (out[name] * factor).astype(out[name].dtype)
    return out
```

```python
from contextlib import ExitStack

import concourse.bass as bass
from concourse import mybir
from concourse.alu_op_type import AluOpType as ALU

F32 = mybir.dt.float32
ACT = mybir.ActivationFunctionType
AX = mybir.AxisListType

B, H, W, C = 2, 256, 256, 256
P = 128
HEADS, HD, Q = 8, 32, 9
GROUPS, GC = 32, 8
LJ, LI = 8, 16
STEPS = 128 // LI
CHUNKS = B * 128 // LJ
CPI = CHUNKS // B
NT = CHUNKS * STEPS
FIRST = 2
JW = 2 * LJ + 1
HK = 3 * HEADS
KP = Q * LJ
ROWS = 2 * LI
NA = Q * 3 * HK
VRING = 9
RES_DMAS = 5
W_DMAS = 8
XV_PIECES = 8
XV_ROWS = 2 * 2 * LJ // XV_PIECES
EPS = 1e-5
SCALE = HD ** -0.5
STAT_W = 32
STAT_TILES = 2 * W // STAT_W


def build(nc, x, conv_wt, attn_wt, attn_b, proj_wt, proj_b, pool_m, avg_m, inner_m, out):
    with ExitStack() as ctx:
        def sb(name, shape):
            return ctx.enter_context(nc.sbuf_tensor(name, shape, F32))

        def ps(name, shape):
            return ctx.enter_context(nc.psum_tensor(name, shape, F32))

        def sem(name):
            return ctx.enter_context(nc.semaphore(name))

        wv = sb("wv", [P, 2, Q, C])
        wa = sb("wa", [P, 2, NA])
        wp = sb("wp", [P, 2, C])
        ab = sb("ab", [P, NA])
        pb = sb("pb", [P, C])
        poolm = sb("poolm", [P, 64])
        inner = sb("inner", [P, CHUNKS])
        mean_c = sb("mean_c", [P, B, C + 1])
        rtok = sb("rtok", [P, B, STEPS, 3])
        cstat = sb("cstat", [P, B, 2, 2])
        nmean = sb("nmean", [P, B, 2])
        vscale = sb("vscale", [P, STEPS, 3])
        pscale = sb("pscale", [P, 2])
        pbias = sb("pbias", [P, 2])
        xv = sb("xv", [P, 2, JW, C + 1])
        xs = sb("xs", [P, 2, 2, 3, JW * LI])
        vtok = sb("vtok", [P, VRING, C])
        vg = sb("vg", [P, 2, LI, C])
        ag = sb("ag", [P, 2, LI, JW * HK])
        tl = sb("tl", [P, NA])
        tmax = sb("tmax", [P, 3 * HK])
        tsum = sb("tsum", [P, 3 * HK])
        trec = sb("trec", [P, 3 * HK])
        yb = sb("yb", [P, 2, 2, JW, ROWS])
        ecarry = sb("ecarry", [P, 2, H])
        res = sb("res", [P, 2, 4, C])
        slab = sb("slab", [P, 4, C])
        pooled = sb("pooled", [P, 2, STEPS, LJ, LI])
        xt = [vg[:].rearrange("p u l c -> p (u l) c"),
              ag[:].rearrange("p u l f -> p (u l f)")[:, 0:STAT_W * C].rearrange("p (w c) -> p w c", c=C)]
        avgm = yb[:].rearrange("p u a j r -> p (u a j r)")[:, 0:P]
        agf = ag[:].rearrange("p u l f -> p (u l f)")[:, STAT_W * C:]
        NB = GROUPS * STAT_TILES * 6
        bn = agf[:, 0:NB].rearrange("p (g t k) -> p g t k", g=GROUPS, k=6)
        mv = agf[:, NB:NB + 2 * GROUPS].rearrange("p (g k) -> p g k", k=2)
        dev = agf[:, NB + 64:NB + 96]
        vpart = agf[:, NB + 96:NB + 128]
        gmean = agf[:, NB + 128:NB + 160]
        gstd = agf[:, NB + 160:NB + 192]
        mpart = agf[:, NB + 192:NB + 224]
        rstd_c = agf[:, NB + 224:NB + 224 + B * (C + 1)].rearrange("p (b c) -> p b c", b=B)

        psv = ps("psv", [P, 2, 2, C])
        psl = ps("psl", [P, 2, 512])
        psy = ps("psy", [P, 2, 512])
        psp = ps("psp", [P, 2, C])
        psx = ps("psx", [P, 2, C])

        scr = nc.dram_tensor("scr_probs", (2, P, NA), F32, kind="Internal").ap()
        sstat = nc.dram_tensor("scr_stat", (B, 2, C + 1), F32, kind="Internal").ap()

        s_w = sem("s_weights")
        s_zero = sem("s_zeroed")
        s_xt = [sem("s_xt0"), sem("s_xt1")]
        s_bn = sem("s_bn")
        s_bnag = sem("s_bn_aggregated")
        s_st = sem("s_stat_vector")
        s_stp = sem("s_stat_pe")
        s_sta = sem("s_stat_act")
        s_std = sem("s_stat_stored")
        s_stl = sem("s_stat_loaded")
        s_vs = sem("s_vscale_set")
        s_ps = sem("s_pscale_set")
        s_xv = sem("s_xv_loaded")
        s_row = sem("s_xv_row0")
        s_xsub = sem("s_xs_sub")
        s_xs = sem("s_xs_ready")
        s_vmm = sem("s_v_products")
        s_vev = sem("s_v_evacuated")
        s_vg = [sem("s_vg0"), sem("s_vg1")]
        s_l = sem("s_logits")
        s_d1 = sem("s_logits_biased")
        s_d2 = sem("s_logits_max")
        s_d3 = sem("s_logits_less_max")
        s_exp = sem("s_exp")
        s_d4 = sem("s_sum")
        s_d5 = sem("s_recip")
        s_p = sem("s_probs")
        s_as = sem("s_probs_stored")
        s_ag = [sem("s_ag0"), sem("s_ag1")]
        s_c = sem("s_combined")
        s_ym = sem("s_y_moved")
        s_ya = sem("s_y_row_added")
        s_pj = sem("s_projected")
        s_rl = [sem("s_res_loaded0"), sem("s_res_loaded1")]
        s_rb = sem("s_res_biased")
        s_ra = sem("s_res_added")
        s_rs = [sem("s_res_stored0"), sem("s_res_stored1")]
        s_e1 = sem("s_edge_summed")
        s_e2 = sem("s_edge_carried")
        s_sl = sem("s_slab_loaded")
        s_um = sem("s_pool_products")
        s_pu = sem("s_pool_evacuated")

        def wait(eng, s, v):
            if isinstance(v, int) and v <= 0:
                return
            eng.wait_ge(s, v)

        def chunk_of(g, u):
            return g + u // STEPS, u % STEPS

        def adds(g, u, h):
            return (2 * STEPS - 1) * g + 2 * u + h - u // STEPS

        def present(g, u, ahead):
            return (not isinstance(g, int)) or 0 <= STEPS * g + u + ahead < NT

        def loop(eng, step):
            for u in range(FIRST):
                step(0, u)
            with eng.Fori(0, CHUNKS - 1) as g:
                for u in range(FIRST, FIRST + STEPS):
                    step(g, u)
            for u in range(FIRST, STEPS + 1):
                step(CHUNKS - 1, u)

        x_pix = x.rearrange("b h w c -> b (h w c)")
        x_rows = x.rearrange("b h w c -> (b h) w c")

        def pixels(a, g, first, count):
            col = (g % CPI) * (2 * LJ * C) + first * C
            return a.rearrange("b h w c -> b h (w c)")[bass.ds(g // CPI, 1), :, bass.ds(col, count * C)]

        block = ctx.enter_context(nc.Block())

        @block.sync
        def _(sp):
            sp.dma_start(avgm, avg_m).then_inc(s_w, 16)
            sp.dma_start(inner[:], inner_m).then_inc(s_w, 16)
            sp.dma_start(poolm[:], pool_m).then_inc(s_w, 16)
            sp.dma_start(wv[:], conv_wt.rearrange("(a p) q o -> p a q o", p=P)).then_inc(s_w, 16)
            sp.dma_start(wa[:], attn_wt.rearrange("(a p) f -> p a f", p=P)).then_inc(s_w, 16)
            sp.dma_start(wp[:], proj_wt.rearrange("(a p) o -> p a o", p=P)).then_inc(s_w, 16)
            sp.dma_start(ab[:], attn_b.partition_broadcast(P)).then_inc(s_w, 16)
            sp.dma_start(pb[:], proj_b.partition_broadcast(P)).then_inc(s_w, 16)

            def load_xv(g, n):
                a, r = n // (XV_PIECES // 2), n % (XV_PIECES // 2) * XV_ROWS
                src = x_rows[bass.ds(g * 2 * LJ + r, XV_ROWS), a * P:(a + 1) * P, :].rearrange("h w c -> w h c")
                sp.dma_start(xv[:, a, 1 + r:1 + r + XV_ROWS, 1:C + 1], src).then_inc(s_xv, 16)

            sp.wait_ge(s_zero, 4)
            for n in range(XV_PIECES):
                load_xv(0, n)

            def stat_tiles(i):
                for k in range(2):
                    wait(sp, s_bn, 2 * i)
                    n = i % (W // STAT_W)
                    src = x.rearrange("b (a h) w c -> (b a) h (w c)", a=2)[
                        bass.ds((i // (W // STAT_W)) * 2 + k, 1), :, bass.ds(n * STAT_W * C, STAT_W * C)]
                    sp.dma_start(xt[k], src.rearrange("o h f -> (o h) f").rearrange(
                        "h (w c) -> h w c", c=C)).then_inc(s_xt[k], 16)

            stat_tiles(0)
            with sp.Fori(1, B * STAT_TILES // 2) as i:
                stat_tiles(i)
            sp.wait_ge(s_st, STAT_DONE)
            sp.dma_start(sstat[:, 0:1], mean_c[0:1]).then_inc(s_std, 16)
            sp.dma_start(sstat[:, 1:2], rstd_c[0:1]).then_inc(s_std, 16)
            sp.wait_ge(s_std, 32)
            with nc.allow_non_contiguous_dma(reason="a few statistics"):
                for b in range(B):
                    for k in range(2):
                        sp.dma_start(cstat[:, b, k, :],
                                     sstat[b, k, 1:C + 1].rearrange("(a c) -> c a", a=2)).then_inc(s_stl, 16)
                    for lj in range(LJ):
                        src = bass.AP(sstat.tensor, (2 * b + 1) * (C + 1), [[2, LI], [2 * LI, STEPS], [1, 3]])
                        sp.dma_start(rtok[LI * lj:LI * lj + LI, b], src).then_inc(s_stl, 16)

            XV_AFTER = {STEPS - 2: ({8: 3}, 0), STEPS - 1: ({1: 1, 3: 1, 5: 2, 7: 1}, 3)}

            def regroup(g, u):
                t = STEPS * g + u
                cg, s = chunk_of(g, u)
                after, piece = XV_AFTER.get(s, ({}, 0)) if present(g, u, STEPS - s) else ({}, 0)
                piece = iter(range(piece, XV_PIECES))
                k = u % 2

                def v_rows(q):
                    wait(sp, s_vev, Q * t + q + 1)
                    slot = (Q * u + q) % VRING
                    src = bass.AP(vtok[:].tensor, slot * C, [[VRING * C, P], [1, C]])
                    dst = vg[q * LJ:(q + 1) * LJ, k]
                    sp.dma_start(dst, src).then_inc(s_vg[k], 16)
                    for _ in range(after.get(q, 0)):
                        if s == STEPS - 2:
                            wait(sp, s_row, cg + 1)
                        load_xv(cg + 1, next(piece))

                wait(sp, s_c, 2 * (t - 1))
                for q in range(6):
                    v_rows(q)
                wait(sp, s_p, t + 1)
                wait(sp, s_ag[k], LJ * 16 * (t // 2))
                sp.dma_start(scr[k], tl[:]).then_inc(s_as, 16)
                v_rows(6)
                v_rows(7)
                wait(sp, s_as, 16 * (t + 1))
                for lj in range(LJ):
                    src = scr[k, LI * lj:LI * lj + LI].rearrange("l (q f) -> q l f", q=Q)
                    sp.dma_start(ag[lj:KP:LJ, k, :, 2 * lj * HK:2 * lj * HK + 3 * HK], src).then_inc(s_ag[k], 16)
                v_rows(8)

            sp.wait_ge(s_zero, 5)
            regroup(0, 0)

            def step(g, u):
                if present(g, u, 1):
                    regroup(g, u + 1)

            loop(sp, step)

        @block.gpsimd
        def _(pool):
            nc.gpsimd.memset(mean_c[:], 0.0).then_inc(s_zero, 1)
            nc.gpsimd.memset(rstd_c, 0.0).then_inc(s_zero, 1)
            nc.gpsimd.memset(ecarry[:], 0.0).then_inc(s_zero, 1)
            nc.gpsimd.memset(xv[:], 0.0).then_inc(s_zero, 1)
            pool.wait_ge(s_w, W_DMAS * 16)
            pool.wait_ge(s_zero, 5)

            def load_slab(g, u):
                t = STEPS * g + u
                cg, n = chunk_of(g, u)
                wait(pool, s_um, t)
                rows = slice((n // 4) * P, (n // 4) * P + P)
                src = pixels(x, cg, 4 * (n % 4), 4)[:, rows].rearrange("o h f -> (o h) f")
                pool.dma_start(slab[:].rearrange("p w c -> p (w c)"), src).then_inc(s_sl, 16)

            def edge_chunk(g):
                return (g + CHUNKS - 1) % CHUNKS

            def res_dma(g, u, store):
                cg, s = chunk_of(g, u)
                k = u % 2
                a = out if store else x
                sems = s_rs[k] if store else s_rl[k]
                rows = slice(ROWS * s, ROWS * s + ROWS)
                edge = pixels(a, edge_chunk(cg), 15, 1)[:, rows].rearrange("o h f -> (o h) f")
                rest = pixels(a, cg, 0, 15)[:, rows]

                def columns(first, dims):
                    v = rest[:, :, first * C:(first + 1) * C]
                    return bass.AP(v.tensor, v.offset, dims + [[1, C]], runtime_checks=v.runtime_checks)

                tiles = [(res[0:ROWS, k, 0], edge),
                         (res[ROWS:P, k, 0], columns(0, [[C, 3], [W * C, ROWS]])),
                         *((res[:, k, n], columns(4 * n - 1, [[C, 4], [W * C, ROWS]])) for n in range(1, 4))]
                for sbuf, dram in tiles:
                    src, dst = (sbuf, dram) if store else (dram, sbuf)
                    pool.dma_start(dst, src).then_inc(sems, 16)

            def bias_res(g, u):
                t = STEPS * g + u
                k = u % 2
                wait(pool, s_rl[k], RES_DMAS * 16 * (t // 2 + 1))
                nc.gpsimd.tensor_tensor(res[:, k], res[:, k], pb[:].unsqueeze(1).broadcast_to([P, 4, C]),
                                        ALU.add).then_inc(s_rb, 1)

            for n in range(6):
                load_slab(0, n)

            def step(g, u):
                t = STEPS * g + u
                if present(g, u, 6):
                    load_slab(g, u + 6)
                if present(g, u, 0):
                    k = u % 2
                    wait(pool, s_rs[k], RES_DMAS * 16 * (t // 2))
                    res_dma(g, u, False)
                if present(g, u, -1):
                    wait(pool, s_ra, 2 * t)
                if present(g, u, 0):
                    bias_res(g, u)
                if present(g, u, -1):
                    res_dma(g, u - 1, True)

            loop(pool, step)
            pool.wait_ge(s_rs[0], RES_DMAS * 16 * (NT // 2))
            last = pixels(x, CHUNKS - 1, 15, 1).rearrange("o (a h) f -> h (o a) f", h=P)
            pool.dma_start(res[:, 0, 0:2], last).then_inc(s_rl[0], 16)
            pool.wait_ge(s_rl[0], RES_DMAS * 16 * (NT // 2) + 16)
            nc.gpsimd.tensor_tensor(res[:, 0, 0:2], res[:, 0, 0:2], pb[:].unsqueeze(1).broadcast_to([P, 2, C]),
                                    ALU.add).then_inc(s_rb, 1)
            pool.wait_ge(s_ra, 2 * NT + 1)
            pool.wait_ge(s_rs[1], RES_DMAS * 16 * (NT // 2))
            last = pixels(out, CHUNKS - 1, 15, 1).rearrange("o (a h) f -> h (o a) f", h=P)
            pool.dma_start(last, res[:, 0, 0:2]).then_inc(s_rs[0], 16)
            pool.wait_ge(s_rs[0], RES_DMAS * 16 * (NT // 2) + 16)

        @block.tensor
        def _(pe):
            pe.wait_ge(s_w, W_DMAS * 16)
            for b in range(B):
                pe.wait_ge(s_st, STAT_STEPS * b + 1)
                nc.tensor.matmul(psx[:, 0, 0:GROUPS], avgm, mpart, start=True, stop=True).then_inc(s_stp, 1)
                pe.wait_ge(s_st, STAT_STEPS * b + 5)
                nc.tensor.matmul(psx[:, 0, 0:GROUPS], avgm, vpart, start=True, stop=True).then_inc(s_stp, 1)

            def v_group(g, u, i):
                t = STEPS * g + u
                k = u % 2
                bank = (5 * u + i) % 2
                if i == 0:
                    wait(pe, s_xs, t + 1)
                wait(pe, s_vev, Q * t + 2 * i - 2 if i >= 2 else Q * (t - 1) + 8 + i)
                for q in range(2 * i, min(2 * i + 2, Q)):
                    ki, kj = q // 3, q % 3
                    for a in range(2):
                        row = (kj % 2) * (LJ + 1) + kj // 2
                        lhs = xs[:, k, a, ki, row * LI:(row + LJ) * LI]
                        mm = nc.tensor.matmul(psv[:, bank, q % 2], lhs, wv[:, a, q], start=(a == 0), stop=(a == 1))
                mm.then_inc(s_vmm, 1)

            def logits(g, u):
                t = STEPS * g + u
                cg, s = chunk_of(g, u)
                wait(pe, s_pu, STEPS * cg + (4 if s < 4 else 8))
                wait(pe, s_d1, t)
                for half in range(2):
                    for a in range(2):
                        lhs = pooled[:, a, s].rearrange("p j i -> p (j i)")
                        mm = nc.tensor.matmul(psl[:, half, 0:NA // 2], lhs, wa[:, a, half * (NA // 2):(half + 1) * (NA // 2)],
                                              start=(a == 0), stop=(a == 1))
                mm.then_inc(s_l, 1)

            def combine(g, u, h):
                t = STEPS * g + u
                cg, s = chunk_of(g, u)
                k = u % 2
                if h == 0:
                    wait(pe, s_vg[k], 16 * Q * (t // 2 + 1))
                    wait(pe, s_ag[k], 16 * LJ * (t // 2 + 1))
                wait(pe, s_ym, 2 * t + h)
                wait(pe, s_ya, adds(g, u, h) - (0 if s == 0 and h == 0 else 1))
                for l in range(8):
                    li = 8 * h + l
                    probs = ag[0:KP, k, li].rearrange("p (j n i) -> p n i j", n=HEADS, i=3)
                    for n in range(HEADS):
                        part = slice(HD * (n % 4), HD * (n % 4) + HD)
                        mm = nc.tensor.matmul(psy[part, n // 4, 2 * l * JW:(2 * l + 3) * JW],
                                              vg[0:KP, k, li, n * HD:(n + 1) * HD], probs[:, n],
                                              start=(l == 0), stop=True, skip_group_check=True)
                mm.then_inc(s_c, 1)

            def project(g, u, p):
                t = STEPS * g + u
                k = u % 2
                wait(pe, s_e1, t + 1)
                wait(pe, s_ra, 2 * t + p)
                for n in range(2):
                    j0 = 4 * (2 * p + n)
                    for a in range(2):
                        lhs = yb[:, k, a, j0:j0 + 4].rearrange("p j r -> p (j r)")
                        mm = nc.tensor.matmul(psp[:, n], lhs, wp[:, a], start=(a == 0), stop=(a == 1))
                mm.then_inc(s_pj, 1)

            def pool_unit(g, u):
                t = STEPS * g + u
                wait(pe, s_sl, 16 * (t + 1))
                wait(pe, s_pu, t)
                for a in range(2):
                    for l in range(2):
                        for w in range(2):
                            mm = nc.tensor.matmul(psx[:, 0, a * P + l * 64:a * P + l * 64 + 64],
                                                  slab[:, 2 * l + w, a * P:(a + 1) * P], poolm[:],
                                                  start=(w == 0), stop=(w == 1))
                mm.then_inc(s_um, 1)

            pe.wait_ge(s_st, STAT_DONE)
            for n in range(6):
                pool_unit(0, n)
            logits(0, 0)
            for i in range(5):
                v_group(0, 0, i)

            def step(g, u):
                t = STEPS * g + u
                ahead, here, behind = present(g, u, 1), present(g, u, 0), present(g, u, -1)
                if ahead:
                    logits(g, u + 1)
                    v_group(g, u + 1, 0)
                    v_group(g, u + 1, 1)
                if here:
                    combine(g, u, 0)
                if ahead:
                    v_group(g, u + 1, 2)
                if behind:
                    project(g, u - 1, 0)
                if ahead:
                    v_group(g, u + 1, 3)
                if here:
                    combine(g, u, 1)
                if ahead:
                    v_group(g, u + 1, 4)
                if behind:
                    project(g, u - 1, 1)
                if present(g, u, 6):
                    pool_unit(g, u + 6)

            loop(pe, step)
            pe.wait_ge(s_e2, NT)
            pe.wait_ge(s_ra, 2 * NT)
            for half in range(2):
                for a in range(2):
                    mm = nc.tensor.matmul(psp[:, half], ecarry[:, a, half * P:(half + 1) * P], wp[:, a],
                                          start=(a == 0), stop=(a == 1))
            mm.then_inc(s_pj, 1)

        @block.scalar
        def _(act):
            for b in range(B):
                act.wait_ge(s_st, STAT_STEPS * b + 6)
                nc.scalar.activation(gstd, gstd, ACT.Sqrt).then_inc(s_sta, 1)

            def v_out(g, u, q):
                t = STEPS * g + u
                cg, s = chunk_of(g, u)
                if q == 0 and s == 0:
                    wait(act, s_vs, cg + 1)
                if q % 2 == 0:
                    wait(act, s_vmm, 5 * t + q // 2 + 1)
                if q == 0:
                    wait(act, s_vg[(u + 1) % 2], 16 * Q * ((t + 1) // 2))
                bank = (5 * u + q // 2) % 2
                nc.scalar.activation(vtok[:, (Q * u + q) % VRING], psv[:, bank, q % 2], ACT.Copy,
                                     scale=vscale[:, s, q // 3:q // 3 + 1]).then_inc(s_vev, 1)

            def exp(g, u):
                t = STEPS * g + u
                wait(act, s_d3, t + 1)
                nc.scalar.activation(tl[:], tl[:], ACT.Exp, scale=SCALE).then_inc(s_exp, 1)

            def pool_out(g, u):
                t = STEPS * g + u
                cg, n = chunk_of(g, u)
                wait(act, s_um, t + 1)
                wait(act, s_l, STEPS * cg + (4 - STEPS if n < 4 else 0))
                if n == 0:
                    wait(act, s_ps, 2 * (cg + 1))
                for a in range(2):
                    last = nc.scalar.activation(
                        pooled[:, a, 4 * (n // 4):4 * (n // 4) + 4, 2 * (n % 4):2 * (n % 4) + 2],
                        psx[:, 0, a * P:(a + 1) * P].rearrange("p (l s i) -> p s l i", l=2, i=LI), ACT.Identity,
                        scale=pscale[:, a:a + 1], bias=pbias[:, a:a + 1])
                last.then_inc(s_pu, 1)

            act.wait_ge(s_stl, 16 * (2 * B + LJ * B))
            for n in range(6):
                pool_out(0, n)
            for q in range(Q):
                v_out(0, 0, q)
                if q == 1:
                    exp(0, 0)

            def step(g, u):
                if present(g, u, 1):
                    for q in range(Q):
                        v_out(g, u + 1, q)
                        if q == 1:
                            exp(g, u + 1)
                if present(g, u, 6):
                    pool_out(g, u + 6)

            loop(act, step)

        @block.vector
        def _(dve):
            def image_stats(b):
                with dve.Fori(b * STAT_TILES // 2, (b + 1) * STAT_TILES // 2) as i:
                    for k in range(2):
                        dve.wait_ge(s_xt[k], 16 * (i + 1))
                        tile = xt[k].rearrange("p w (g c) -> p g w c", g=GROUPS)
                        for n in range(GROUPS):
                            last = nc.vector.bn_stats(
                                bn[:, n, bass.ds(2 * (i - b * STAT_TILES // 2) + k, 1)].rearrange("p a k -> p (a k)"),
                                tile[:, n])
                        last.then_inc(s_bn, 1)
                base = STAT_STEPS * b
                dve.wait_ge(s_bn, STAT_TILES * (b + 1))
                for n in range(GROUPS):
                    last = nc.vector.bn_aggr(mv[:, n], bn[:, n].rearrange("p t k -> p (t k)"))
                last.then_inc(s_bnag, 1)
                dve.wait_ge(s_bnag, b + 1)
                nc.vector.tensor_copy(mpart, mv[:, :, 0]).then_inc(s_st, 1)
                dve.wait_ge(s_stp, 2 * b + 1)
                nc.vector.tensor_copy(gmean, psx[:, 0, 0:GROUPS]).then_inc(s_st, 1)
                dve.wait_ge(s_st, base + 2)
                nc.vector.tensor_tensor(dev, mpart, gmean, ALU.subtract).then_inc(s_st, 1)
                dve.wait_ge(s_st, base + 3)
                nc.vector.tensor_tensor(dev, dev, dev, ALU.mult).then_inc(s_st, 1)
                dve.wait_ge(s_st, base + 4)
                nc.vector.tensor_tensor(vpart, dev, mv[:, :, 1], ALU.add).then_inc(s_st, 1)
                dve.wait_ge(s_stp, 2 * b + 2)
                nc.vector.tensor_scalar(gstd, psx[:, 0, 0:GROUPS], EPS, None, ALU.add).then_inc(s_st, 1)
                dve.wait_ge(s_sta, b + 1)
                nc.vector.reciprocal(gstd, gstd).then_inc(s_st, 1)
                dve.wait_ge(s_st, base + 7)
                for dst, src in ((mean_c, gmean), (rstd_c, gstd)):
                    nc.vector.tensor_copy(dst[:, b, 1:C + 1].rearrange("p (g c) -> p g c", c=GC),
                                          src.unsqueeze(2).broadcast_to([P, GROUPS, GC])).then_inc(s_st, 1)
                dve.wait_ge(s_st, base + STAT_STEPS)

            dve.wait_ge(s_zero, 4)
            for b in range(B):
                image_stats(b)
            dve.wait_ge(s_std, 32)
            nc.vector.memset(ag[:], 0.0).then_inc(s_zero, 1)
            dve.wait_ge(s_stl, 16 * (2 * B + LJ * B))
            nc.vector.tensor_tensor(nmean[:], cstat[:, :, 0], cstat[:, :, 1], ALU.mult).then_inc(s_st, 1)
            dve.wait_ge(s_st, STAT_DONE + 1)
            nc.vector.tensor_scalar(nmean[:], nmean[:], -1.0, None, ALU.mult).then_inc(s_st, 1)
            dve.wait_ge(s_w, W_DMAS * 16)

            by_q = tl[:].rearrange("p (q f) -> p q f", q=Q)
            by_f = tl[:].rearrange("p (q f) -> p f q", q=Q)

            def over_q(a):
                return a[:].unsqueeze(1).broadcast_to([P, Q, 3 * HK])

            def softmax_in(g, u):
                t = STEPS * g + u
                wait(dve, s_l, t + 1)
                wait(dve, s_as, 16 * t)
                nc.vector.tensor_tensor(tl[:].rearrange("p (a f) -> p a f", a=2), psl[:, :, 0:NA // 2],
                                        ab[:].rearrange("p (a f) -> p a f", a=2), ALU.add).then_inc(s_d1, 1)
                dve.wait_ge(s_d1, t + 1)
                nc.vector.tensor_reduce(tmax[:], by_f, AX.X, ALU.max).then_inc(s_d2, 1)
                dve.wait_ge(s_d2, t + 1)
                nc.vector.tensor_tensor(by_q, by_q, over_q(tmax), ALU.subtract).then_inc(s_d3, 1)

            def softmax_out(g, u):
                t = STEPS * g + u
                dve.wait_ge(s_exp, t + 1)
                nc.vector.tensor_reduce(tsum[:], by_f, AX.X, ALU.add).then_inc(s_d4, 1)
                dve.wait_ge(s_d4, t + 1)
                nc.vector.reciprocal(trec[:], tsum[:]).then_inc(s_d5, 1)
                dve.wait_ge(s_d5, t + 1)
                nc.vector.tensor_tensor(by_q, by_q, over_q(trec), ALU.mult).then_inc(s_p, 1)

            def y_out(g, u, h):
                t = STEPS * g + u
                cg, s = chunk_of(g, u)
                k = u % 2
                wait(dve, s_c, 2 * t + h + 1)
                if h == 0:
                    wait(dve, s_pj, 2 * (t - 1))
                    wait(dve, s_e2, t - 1)
                nc.vector.tensor_copy(yb[:, k, :, :, 16 * h:16 * h + 16],
                                      psy[:, :, JW:17 * JW].rearrange("p a (r j) -> p a j r", j=JW)).then_inc(s_ym, 1)
                if s == 0 and h == 0:
                    return
                row = yb[:, k, :, :, 15] if h else yb[:, (u + 1) % 2, :, :, ROWS - 1]
                dve.wait_ge(s_ym, 2 * t + h)
                nc.vector.tensor_tensor(row, psy[:, :, 0:JW], row, ALU.add).then_inc(s_ya, 1)

            def edges(g, u):
                t = STEPS * g + u
                cg, s = chunk_of(g, u)
                k = u % 2
                rows = slice(ROWS * s, ROWS * s + ROWS)
                wait(dve, s_ym, 2 * t + 2)
                wait(dve, s_ya, adds(g, u + 1, 0))
                wait(dve, s_e2, t)
                nc.vector.scalar_tensor_tensor(out=yb[:, k, :, 0], in0=yb[:, k, :, 0],
                                               scalar=inner[:, bass.ds(cg, 1)], in1=ecarry[:, :, rows],
                                               op0=ALU.mult, op1=ALU.add).then_inc(s_e1, 1)
                dve.wait_ge(s_e1, t + 1)
                nc.vector.tensor_copy(ecarry[:, :, rows], yb[:, k, :, JW - 1]).then_inc(s_e2, 1)

            def res_add(g, u, p):
                t = STEPS * g + u
                k = u % 2
                dve.wait_ge(s_rb, t + 1)
                dve.wait_ge(s_pj, 2 * t + p + 1)
                tiles = res[:, k, 2 * p:2 * p + 2]
                nc.vector.tensor_tensor(tiles, psp[:], tiles, ALU.add).then_inc(s_ra, 1)

            def slice_xs(g, u):
                t = STEPS * g + u
                cg, s = chunk_of(g, u)
                k = u % 2
                if s == 0:
                    wait(dve, s_xv, 16 * XV_PIECES * (cg + 1))
                wait(dve, s_vmm, 5 * (t - 1))
                lo = 2 * LI * s
                mean = mean_c[:, bass.ds(cg // CPI, 1), lo:lo + 2 * LI + 1]
                for a in range(2):
                    for odd in range(2):
                        rows = LJ + 1 - odd
                        src = xv[:, a, odd:JW:2, lo:lo + 2 * LI + 1]
                        src = bass.AP(src.tensor, src.offset, [list(src.ap[0]), [1, 3], list(src.ap[1]), [2, LI]])
                        sub = bass.AP(mean.tensor, mean.offset, [list(mean.ap[0]), [1, 3], [0, rows], [2, LI]])
                        dst = xs[:, k, a, :, odd * (LJ + 1) * LI:(odd * (LJ + 1) + rows) * LI]
                        nc.vector.tensor_tensor(dst.rearrange("p i (r l) -> p i r l", l=LI), src, sub,
                                                ALU.subtract).then_inc(s_xsub, 1)
                wait(dve, s_xsub, 4 * (t + 1))
                m = inner[:, bass.ds(cg, 1)].unsqueeze(2).broadcast_to([P, 6, LI])
                row = xs[:, k].rearrange("p a i f -> p (a i) f")[:, :, 0:LI]
                nc.vector.tensor_tensor(row, row, m, ALU.mult).then_inc(s_xs, 1)

            def next_row0(g, u):
                wait(dve, s_xsub, 4 * (STEPS * g + u + 1))
                nc.vector.tensor_copy(xv[:, :, 0], xv[:, :, JW - 1]).then_inc(s_row, 1)

            def set_vscale(g, u):
                cg = chunk_of(g, u)[0]
                wait(dve, s_vev, Q * STEPS * cg)
                nc.vector.tensor_copy(vscale[:], rtok[:, bass.ds(cg // CPI, 1)].rearrange(
                    "p a s k -> p (a s) k")).then_inc(s_vs, 1)

            def set_pscale(g, u):
                cg = chunk_of(g, u)[0]
                wait(dve, s_pu, STEPS * cg)
                where = bass.ds(cg // CPI, 1)
                nc.vector.tensor_copy(pscale[:], cstat[:, where, 1].rearrange("p a k -> p (a k)")).then_inc(s_ps, 1)
                nc.vector.tensor_copy(pbias[:], nmean[:, where].rearrange("p a k -> p (a k)")).then_inc(s_ps, 1)

            dve.wait_ge(s_st, STAT_DONE + 2)
            set_vscale(0, 0)
            set_pscale(0, 0)
            slice_xs(0, 0)
            slice_xs(0, 1)
            softmax_in(0, 0)
            softmax_out(0, 0)

            def step(g, u):
                ahead, here, behind = present(g, u, 1), present(g, u, 0), present(g, u, -1)
                if u == STEPS - 1 and ahead:
                    set_vscale(g, u + 1)
                if u == 2 and present(g, u, 6):
                    set_pscale(g, u + 6)
                if ahead:
                    softmax_in(g, u + 1)
                if here:
                    y_out(g, u, 0)
                if behind:
                    edges(g, u - 1)
                if ahead:
                    softmax_out(g, u + 1)
                late = (u + 2) % STEPS == 0
                if present(g, u, 2) and not late:
                    slice_xs(g, u + 2)
                if u == 5 and present(g, u, 3):
                    next_row0(g, u + 2)
                if behind:
                    res_add(g, u - 1, 0)
                if here:
                    y_out(g, u, 1)
                if behind:
                    res_add(g, u - 1, 1)
                if present(g, u, 2) and late:
                    slice_xs(g, u + 2)

            loop(dve, step)
            dve.wait_ge(s_rb, NT + 1)
            dve.wait_ge(s_pj, 2 * NT + 1)
            nc.vector.tensor_tensor(res[:, 0, 0:2], psp[:], res[:, 0, 0:2], ALU.add).then_inc(s_ra, 1)


STAT_STEPS = 9
STAT_DONE = STAT_STEPS * B


def kernel(**inputs):
    import numpy as np
    import concourse.bacc as bacc
    from concourse.bass_utils import run_bass_kernel_spmd

    conv_wt = np.asarray(inputs["L0_conv_conv_w"]).reshape(Q, C, C).transpose(2, 0, 1)
    attn_wt = np.asarray(inputs["L0_conv_attn_w"]).reshape(HEADS, 3, 3, Q, C).transpose(4, 3, 2, 0, 1).reshape(C, NA)
    attn_b = np.asarray(inputs["L0_conv_attn_b"]).reshape(HEADS, 3, 3, Q).transpose(3, 2, 0, 1).reshape(NA)
    h = np.arange(P)
    arrays = {
        "x": np.asarray(inputs["x"]), "conv_wt": conv_wt, "attn_wt": attn_wt, "attn_b": attn_b,
        "proj_wt": np.asarray(inputs["L0_conv_proj_w"]).T, "proj_b": np.asarray(inputs["L0_conv_proj_b"]),
        "pool_m": np.where(h[:, None] // 2 == np.arange(64)[None], 0.25, 0.0).astype(np.float32),
        "avg_m": np.full((P, P), 1.0 / P, np.float32),
        "inner_m": np.where(np.arange(CHUNKS) % CPI == 0, 0.0, 1.0).astype(np.float32)[None].repeat(P, 0),
    }
    arrays = {f"in_{k}": np.ascontiguousarray(v) for k, v in arrays.items()}
    nc = bacc.Bacc("TRN2", target_bir_lowering=False, num_devices=1)
    args = [nc.dram_tensor(k, v.shape, F32, kind="ExternalInput").ap() for k, v in arrays.items()]
    out = nc.dram_tensor("out_y", (B, H, W, C), F32, kind="ExternalOutput").ap()
    build(nc, *args, out)
    r = run_bass_kernel_spmd(nc, [arrays], core_ids=[0])
    return r.results[0]["out_y"]
```

```python
from contextlib import ExitStack

import concourse.bass as bass
from concourse import mybir
from concourse.alu_op_type import AluOpType as ALU

F32 = mybir.dt.float32
F32R = mybir.dt.float32r
ACT = mybir.ActivationFunctionType
AX = mybir.AxisListType

B, H, W, C = 2, 256, 256, 256
P = 128
HEADS, HD, Q = 8, 32, 9
GROUPS, GC = 32, 8
LJ, LI = 8, 16
STEPS = 128 // LI
CHUNKS = B * 128 // LJ
CPI = CHUNKS // B
NT = CHUNKS * STEPS
FIRST = 2
JW = 2 * LJ + 1
HK = 3 * HEADS
KP = Q * LJ
ROWS = 2 * LI
NA = Q * 3 * HK
VRING = 9
RES_DMAS = 5
W_DMAS = 7
XV_PIECES = 8
XV_ROWS = 2 * 2 * LJ // XV_PIECES
EPS = 1e-5
SCALE = HD ** -0.5
STAT_W = 32
STAT_TILES = 2 * W // STAT_W


def build(nc, x, conv_wt, attn_wt, attn_b, proj_wt, proj_b, pool_m, avg_m, inner_m, out):
    with ExitStack() as ctx:
        def sb(name, shape):
            return ctx.enter_context(nc.sbuf_tensor(name, shape, F32))

        def ps(name, shape):
            return ctx.enter_context(nc.psum_tensor(name, shape, F32))

        def sem(name):
            return ctx.enter_context(nc.semaphore(name))

        wvh = ctx.enter_context(nc.sbuf_tensor("wvh", [P, 2, Q, C], F32R))
        wvl = ctx.enter_context(nc.sbuf_tensor("wvl", [P, 2, Q, C], F32R))
        wa = sb("wa", [P, 2, NA])
        wp = sb("wp", [P, 2, C])
        ab = sb("ab", [P, NA])
        pb = sb("pb", [P, C])
        poolm = sb("poolm", [P, 64])
        inner = sb("inner", [P, CHUNKS])
        gmean = sb("gmean", [P, B, GROUPS])
        rtok = sb("rtok", [P, B, STEPS, 3])
        cstat = sb("cstat", [P, B, 2, 2])
        nmean = sb("nmean", [P, B, 2])
        vscale = sb("vscale", [P, STEPS, 3])
        pscale = sb("pscale", [P, 2])
        pbias = sb("pbias", [P, 2])
        xv = sb("xv", [P, 2, JW, C + 1])
        xsh = ctx.enter_context(nc.sbuf_tensor("xsh", [P, 2, 2, 3, JW * LI], F32R))
        xsl = ctx.enter_context(nc.sbuf_tensor("xsl", [P, 2, 2, 3, JW * LI], F32R))
        vtok = sb("vtok", [P, VRING, C])
        vg = sb("vg", [P, 2, LI, C])
        ag = sb("ag", [P, LI, JW * HK])
        tl = sb("tl", [P, NA])
        tmax = sb("tmax", [P, 3 * HK])
        tsum = sb("tsum", [P, 3 * HK])
        trec = sb("trec", [P, 3 * HK])
        yb = sb("yb", [P, 2, 2, JW, ROWS])
        ecarry = sb("ecarry", [P, 2, H])
        res = sb("res", [P, 2, 4, C])
        slab = sb("slab", [P, 4, C])
        pooled = sb("pooled", [P, 2, STEPS, LJ, LI])
        xvf = xv[:].rearrange("p a r c -> p (a r c)")
        xt = [vg[:].rearrange("p u l c -> p (u l) c"),
              xvf[:, 0:STAT_W * C].rearrange("p (w c) -> p w c", c=C)]
        wvt = xvf[:, 0:2 * Q * C].rearrange("p (a q c) -> p a q c", a=2, q=Q)
        avgm = yb[:].rearrange("p u a j r -> p (u a j r)")[:, 0:P]
        agf = ag[:].rearrange("p l f -> p (l f)")
        NB = GROUPS * STAT_TILES * 6
        bn = agf[:, 0:NB].rearrange("p (g t k) -> p g t k", g=GROUPS, k=6)
        mv = agf[:, NB:NB + 2 * GROUPS].rearrange("p (g k) -> p g k", k=2)
        dev = agf[:, NB + 64:NB + 96]
        vpart = agf[:, NB + 96:NB + 128]
        gstd = agf[:, NB + 160:NB + 192]
        mpart = agf[:, NB + 192:NB + 224]
        NS = B * (C + 1)
        vtf = vtok[:].rearrange("p r c -> p (r c)")
        mean_c, rstd_c = (vtf[:, n * NS:(n + 1) * NS].rearrange("p (b c) -> p b c", b=B) for n in range(2))

        psv = ps("psv", [P, 2, 2, C])
        psl = ps("psl", [P, 2, 512])
        psy = ps("psy", [P, 2, 512])
        psp = ps("psp", [P, 2, C])
        psx = ps("psx", [P, 2, C])

        scr = nc.dram_tensor("scr_probs", (2, P, NA), F32, kind="Internal").ap()
        sstat = nc.dram_tensor("scr_stat", (B, 2, C + 1), F32, kind="Internal").ap()

        s_w = sem("s_weights")
        s_zero = sem("s_zeroed")
        s_xt = [sem("s_xt0"), sem("s_xt1")]
        s_bn = sem("s_bn")
        s_bnag = sem("s_bn_aggregated")
        s_st = sem("s_stat_vector")
        s_stp = sem("s_stat_pe")
        s_sta = sem("s_stat_act")
        s_std = sem("s_stat_stored")
        s_stl = sem("s_stat_loaded")
        s_vs = sem("s_vscale_set")
        s_ps = sem("s_pscale_set")
        s_xv = sem("s_xv_loaded")
        s_row = sem("s_xv_row0")
        s_w2 = sem("s_conv_weights")
        s_wh = sem("s_conv_weights_hi")
        s_wl = sem("s_conv_weights_lo")
        s_xm = sem("s_xv_less_mean")
        s_xh = sem("s_xs_hi")
        s_xs = sem("s_xs_lo")
        s_vmm = sem("s_v_products")
        s_vev = sem("s_v_evacuated")
        s_vg = [sem("s_vg0"), sem("s_vg1")]
        s_l = sem("s_logits")
        s_d1 = sem("s_logits_biased")
        s_d2 = sem("s_logits_max")
        s_d3 = sem("s_logits_less_max")
        s_exp = sem("s_exp")
        s_d4 = sem("s_sum")
        s_d5 = sem("s_recip")
        s_p = sem("s_probs")
        s_as = sem("s_probs_stored")
        s_ag = sem("s_ag")
        s_c = sem("s_combined")
        s_ym = sem("s_y_moved")
        s_ya = sem("s_y_row_added")
        s_pj = sem("s_projected")
        s_rl = [sem("s_res_loaded0"), sem("s_res_loaded1")]
        s_rb = sem("s_res_biased")
        s_ra = sem("s_res_added")
        s_rs = [sem("s_res_stored0"), sem("s_res_stored1")]
        s_e1 = sem("s_edge_summed")
        s_e2 = sem("s_edge_carried")
        s_sl = sem("s_slab_loaded")
        s_sp = sem("s_slab_paired")
        s_um = sem("s_pool_products")
        s_pu = sem("s_pool_evacuated")

        def wait(eng, s, v):
            if isinstance(v, int) and v <= 0:
                return
            eng.wait_ge(s, v)

        def chunk_of(g, u):
            return g + u // STEPS, u % STEPS

        def adds(g, u, h):
            return (2 * STEPS - 1) * g + 2 * u + h - u // STEPS

        def present(g, u, ahead):
            return (not isinstance(g, int)) or 0 <= STEPS * g + u + ahead < NT

        def loop(eng, step):
            for u in range(FIRST):
                step(0, u)
            with eng.Fori(0, CHUNKS - 1) as g:
                for u in range(FIRST, FIRST + STEPS):
                    step(g, u)
            for u in range(FIRST, STEPS + 1):
                step(CHUNKS - 1, u)

        x_pix = x.rearrange("b h w c -> b (h w c)")
        x_rows = x.rearrange("b h w c -> (b h) w c")

        def pixels(a, g, first, count):
            col = (g % CPI) * (2 * LJ * C) + first * C
            return a.rearrange("b h w c -> b h (w c)")[bass.ds(g // CPI, 1), :, bass.ds(col, count * C)]

        block = ctx.enter_context(nc.Block())

        @block.sync
        def _(sp):
            sp.dma_start(avgm, avg_m).then_inc(s_w, 16)
            sp.dma_start(inner[:], inner_m).then_inc(s_w, 16)
            sp.dma_start(poolm[:], pool_m).then_inc(s_w, 16)
            sp.dma_start(wvt, conv_wt.rearrange("(a p) q o -> p a q o", p=P)).then_inc(s_w2, 16)
            sp.dma_start(wa[:], attn_wt.rearrange("(a p) f -> p a f", p=P)).then_inc(s_w, 16)
            sp.dma_start(wp[:], proj_wt.rearrange("(a p) o -> p a o", p=P)).then_inc(s_w, 16)
            sp.dma_start(ab[:], attn_b.partition_broadcast(P)).then_inc(s_w, 16)
            sp.dma_start(pb[:], proj_b.partition_broadcast(P)).then_inc(s_w, 16)

            def load_xv(g, n):
                a, r = n // (XV_PIECES // 2), n % (XV_PIECES // 2) * XV_ROWS
                src = x_rows[bass.ds(g * 2 * LJ + r, XV_ROWS), a * P:(a + 1) * P, :].rearrange("h w c -> w h c")
                sp.dma_start(xv[:, a, 1 + r:1 + r + XV_ROWS, 1:C + 1], src).then_inc(s_xv, 16)

            def stat_tiles(i):
                for k in range(2):
                    if not (isinstance(i, int) and i == 0):
                        sp.wait_ge(s_bn, 2 * i - 1 + k)
                    elif k == 1:
                        sp.wait_ge(s_wh, 1)
                        sp.wait_ge(s_wl, 1)
                    n = i % (W // STAT_W)
                    src = x.rearrange("b (a h) w c -> (b a) h (w c)", a=2)[
                        bass.ds((i // (W // STAT_W)) * 2 + k, 1), :, bass.ds(n * STAT_W * C, STAT_W * C)]
                    sp.dma_start(xt[k], src.rearrange("o h f -> (o h) f").rearrange(
                        "h (w c) -> h w c", c=C)).then_inc(s_xt[k], 16)

            stat_tiles(0)
            with sp.Fori(1, B * STAT_TILES // 2) as i:
                stat_tiles(i)
            sp.wait_ge(s_st, STAT_DONE)
            sp.dma_start(sstat[:, 0:1], mean_c[0:1]).then_inc(s_std, 16)
            sp.dma_start(sstat[:, 1:2], rstd_c[0:1]).then_inc(s_std, 16)
            for n in range(XV_PIECES):
                load_xv(0, n)
            sp.wait_ge(s_std, 32)
            with nc.allow_non_contiguous_dma(reason="a few statistics"):
                for b in range(B):
                    for k in range(2):
                        sp.dma_start(cstat[:, b, k, :],
                                     sstat[b, k, 1:C + 1].rearrange("(a c) -> c a", a=2)).then_inc(s_stl, 16)
                    for lj in range(LJ):
                        src = bass.AP(sstat.tensor, (2 * b + 1) * (C + 1), [[2, LI], [2 * LI, STEPS], [1, 3]])
                        sp.dma_start(rtok[LI * lj:LI * lj + LI, b], src).then_inc(s_stl, 16)

            def regroup_v(g, u):
                t = STEPS * g + u
                cg, s = chunk_of(g, u)
                k = u % 2
                pieces = {}
                if s == STEPS - 2 and present(g, u, 2):
                    pieces = {4: range(XV_PIECES // 2)}
                if s == STEPS - 1 and present(g, u, 1):
                    pieces = {0: range(XV_PIECES // 2, XV_PIECES)}
                for q in range(Q):
                    wait(sp, s_vev, Q * t + q + 1)
                    slot = (Q * u + q) % VRING
                    src = bass.AP(vtok[:].tensor, slot * C, [[VRING * C, P], [1, C]])
                    sp.dma_start(vg[q * LJ:(q + 1) * LJ, k], src).then_inc(s_vg[k], 16)
                    for n in pieces.get(q, ()):
                        if n == 0:
                            wait(sp, s_row, cg + 1)
                        load_xv(cg + 1, n)

            def regroup_probs(g, u):
                t = STEPS * g + u
                k = u % 2
                wait(sp, s_p, t + 1)
                sp.dma_start(scr[k], tl[:]).then_inc(s_as, 16)
                wait(sp, s_as, 16 * (t + 1))
                wait(sp, s_c, 16 * (t + 1))
                for lj in range(LJ):
                    src = scr[k, LI * lj:LI * lj + LI].rearrange("l (q f) -> q l f", q=Q)
                    sp.dma_start(ag[lj:KP:LJ, :, 2 * lj * HK:2 * lj * HK + 3 * HK], src).then_inc(s_ag, 16)

            regroup_v(0, 0)
            regroup_probs(0, 0)
            regroup_v(0, 1)

            def step(g, u):
                if present(g, u, 1):
                    regroup_probs(g, u + 1)
                if present(g, u, 2):
                    regroup_v(g, u + 2)

            loop(sp, step)

        @block.gpsimd
        def _(pool):
            nc.gpsimd.memset(vtf[:, 0:2 * NS], 0.0).then_inc(s_zero, 1)
            nc.gpsimd.memset(ecarry[:], 0.0).then_inc(s_zero, 1)
            pool.wait_ge(s_w, W_DMAS * 16)
            pool.wait_ge(s_zero, 4)

            def load_slab(g, u):
                t = STEPS * g + u
                cg, n = chunk_of(g, u)
                wait(pool, s_um, t)
                rows = slice((n // 4) * P, (n // 4) * P + P)
                src = pixels(x, cg, 4 * (n % 4), 4)[:, rows].rearrange("o h f -> (o h) f")
                pool.dma_start(slab[:].rearrange("p w c -> p (w c)"), src).then_inc(s_sl, 16)

            def edge_chunk(g):
                return (g + CHUNKS - 1) % CHUNKS

            def res_dma(g, u, store):
                cg, s = chunk_of(g, u)
                k = u % 2
                a = out if store else x
                sems = s_rs[k] if store else s_rl[k]
                rows = slice(ROWS * s, ROWS * s + ROWS)
                edge = pixels(a, edge_chunk(cg), 15, 1)[:, rows].rearrange("o h f -> (o h) f")
                rest = pixels(a, cg, 0, 15)[:, rows]

                def columns(first, dims):
                    v = rest[:, :, first * C:(first + 1) * C]
                    return bass.AP(v.tensor, v.offset, dims + [[1, C]], runtime_checks=v.runtime_checks)

                tiles = [(res[0:ROWS, k, 0], edge),
                         (res[ROWS:P, k, 0], columns(0, [[C, 3], [W * C, ROWS]])),
                         *((res[:, k, n], columns(4 * n - 1, [[C, 4], [W * C, ROWS]])) for n in range(1, 4))]
                for sbuf, dram in tiles:
                    src, dst = (sbuf, dram) if store else (dram, sbuf)
                    pool.dma_start(dst, src).then_inc(sems, 16)

            def bias_res(g, u):
                t = STEPS * g + u
                k = u % 2
                wait(pool, s_rl[k], RES_DMAS * 16 * (t // 2 + 1))
                nc.gpsimd.tensor_tensor(res[:, k], res[:, k], pb[:].unsqueeze(1).broadcast_to([P, 4, C]),
                                        ALU.add).then_inc(s_rb, 1)

            for n in range(6):
                load_slab(0, n)

            def step(g, u):
                t = STEPS * g + u
                if present(g, u, 6):
                    load_slab(g, u + 6)
                if present(g, u, 0):
                    k = u % 2
                    wait(pool, s_rs[k], RES_DMAS * 16 * (t // 2))
                    res_dma(g, u, False)
                if present(g, u, -1):
                    wait(pool, s_ra, 2 * t)
                if present(g, u, 0):
                    bias_res(g, u)
                if present(g, u, -1):
                    res_dma(g, u - 1, True)

            loop(pool, step)
            pool.wait_ge(s_rs[0], RES_DMAS * 16 * (NT // 2))
            last = pixels(x, CHUNKS - 1, 15, 1).rearrange("o (a h) f -> h (o a) f", h=P)
            pool.dma_start(res[:, 0, 0:2], last).then_inc(s_rl[0], 16)
            pool.wait_ge(s_rl[0], RES_DMAS * 16 * (NT // 2) + 16)
            nc.gpsimd.tensor_tensor(res[:, 0, 0:2], res[:, 0, 0:2], pb[:].unsqueeze(1).broadcast_to([P, 2, C]),
                                    ALU.add).then_inc(s_rb, 1)
            pool.wait_ge(s_ra, 2 * NT + 1)
            pool.wait_ge(s_rs[1], RES_DMAS * 16 * (NT // 2))
            last = pixels(out, CHUNKS - 1, 15, 1).rearrange("o (a h) f -> h (o a) f", h=P)
            pool.dma_start(last, res[:, 0, 0:2]).then_inc(s_rs[0], 16)
            pool.wait_ge(s_rs[0], RES_DMAS * 16 * (NT // 2) + 16)

        @block.tensor
        def _(pe):
            pe.wait_ge(s_w, W_DMAS * 16)
            for b in range(B):
                pe.wait_ge(s_st, STAT_STEPS * b + 1)
                nc.tensor.matmul(psx[:, 0, 0:GROUPS], avgm, mpart, start=True, stop=True).then_inc(s_stp, 1)
                pe.wait_ge(s_st, STAT_STEPS * b + 5)
                nc.tensor.matmul(psx[:, 0, 0:GROUPS], avgm, vpart, start=True, stop=True).then_inc(s_stp, 1)

            def v_group(g, u, i):
                t = STEPS * g + u
                k = u % 2
                bank = (5 * u + i) % 2
                if i == 0:
                    wait(pe, s_xs, t + 1)
                wait(pe, s_vev, Q * t + 2 * i - 2 if i >= 2 else Q * (t - 1) + 8 + i)
                for q in range(2 * i, min(2 * i + 2, Q)):
                    ki, kj = q // 3, q % 3
                    row = (kj % 2) * (LJ + 1) + kj // 2
                    terms = [(x_part, w_part, a) for a in range(2)
                             for x_part, w_part in ((xsl, wvh), (xsh, wvl), (xsh, wvh))]
                    for n, (x_part, w_part, a) in enumerate(terms):
                        mm = nc.tensor.matmul(psv[:, bank, q % 2], x_part[:, k, a, ki, row * LI:(row + LJ) * LI],
                                              w_part[:, a, q], start=(n == 0), stop=(n == len(terms) - 1))
                mm.then_inc(s_vmm, 1)

            def logits(g, u):
                t = STEPS * g + u
                cg, s = chunk_of(g, u)
                wait(pe, s_pu, STEPS * cg + (4 if s < 4 else 8))
                wait(pe, s_d1, t)
                for half in range(2):
                    for a in range(2):
                        lhs = pooled[:, a, s].rearrange("p j i -> p (j i)")
                        mm = nc.tensor.matmul(psl[:, half, 0:NA // 2], lhs, wa[:, a, half * (NA // 2):(half + 1) * (NA // 2)],
                                              start=(a == 0), stop=(a == 1))
                mm.then_inc(s_l, 1)

            def combine(g, u, h):
                t = STEPS * g + u
                cg, s = chunk_of(g, u)
                k = u % 2
                if h == 0:
                    wait(pe, s_vg[k], 16 * Q * (t // 2 + 1))
                    wait(pe, s_ag, 16 * LJ * (t + 1))
                wait(pe, s_ym, 2 * t + h)
                wait(pe, s_ya, adds(g, u, h) - (0 if s == 0 and h == 0 else 1))
                for l in range(8):
                    li = 8 * h + l
                    probs = ag[0:KP, li].rearrange("p (j n i) -> p n i j", n=HEADS, i=3)
                    for n in range(HEADS):
                        part = slice(HD * (n % 4), HD * (n % 4) + HD)
                        mm = nc.tensor.matmul(psy[part, n // 4, 2 * l * JW:(2 * l + 3) * JW],
                                              vg[0:KP, k, li, n * HD:(n + 1) * HD], probs[:, n],
                                              start=(l == 0), stop=True, skip_group_check=True)
                mm.then_inc(s_c, 8)

            def project(g, u, p):
                t = STEPS * g + u
                k = u % 2
                wait(pe, s_e1, t + 1)
                wait(pe, s_ra, 2 * t + p)
                for n in range(2):
                    j0 = 4 * (2 * p + n)
                    for a in range(2):
                        lhs = yb[:, k, a, j0:j0 + 4].rearrange("p j r -> p (j r)")
                        mm = nc.tensor.matmul(psp[:, n], lhs, wp[:, a], start=(a == 0), stop=(a == 1))
                mm.then_inc(s_pj, 1)

            def pool_unit(g, u):
                t = STEPS * g + u
                wait(pe, s_sp, t + 1)
                wait(pe, s_pu, t)
                for a in range(2):
                    for l in range(2):
                        mm = nc.tensor.matmul(psx[:, 0, a * P + l * 64:a * P + l * 64 + 64],
                                              slab[:, 2 * l, a * P:(a + 1) * P], poolm[:], start=True, stop=True)
                mm.then_inc(s_um, 1)

            pe.wait_ge(s_st, STAT_DONE)
            pe.wait_ge(s_wl, 1)
            pool_unit(0, 0)
            for i in range(2):
                v_group(0, 0, i)
            pool_unit(0, 1)
            for i in range(2, 5):
                v_group(0, 0, i)
            pool_unit(0, 2)
            for i in range(2):
                v_group(0, 1, i)
            pool_unit(0, 3)
            logits(0, 0)
            for i in range(2, 5):
                v_group(0, 1, i)
            pool_unit(0, 4)
            pool_unit(0, 5)
            logits(0, 1)

            def step(g, u):
                t = STEPS * g + u
                ahead, here, behind = present(g, u, 2), present(g, u, 0), present(g, u, -1)
                late = (u + 2) % STEPS == 0
                if here:
                    combine(g, u, 0)
                if ahead:
                    if late:
                        logits(g, u + 2)
                    else:
                        v_group(g, u + 2, 0)
                if here:
                    combine(g, u, 1)
                if ahead and not late:
                    v_group(g, u + 2, 1)
                if behind:
                    project(g, u - 1, 0)
                if ahead:
                    if late:
                        v_group(g, u + 2, 0)
                        v_group(g, u + 2, 1)
                    else:
                        logits(g, u + 2)
                    v_group(g, u + 2, 2)
                    v_group(g, u + 2, 3)
                if present(g, u, 6):
                    pool_unit(g, u + 6)
                if behind:
                    project(g, u - 1, 1)
                if ahead:
                    v_group(g, u + 2, 4)

            loop(pe, step)
            pe.wait_ge(s_e2, NT)
            pe.wait_ge(s_ra, 2 * NT)
            for half in range(2):
                for a in range(2):
                    mm = nc.tensor.matmul(psp[:, half], ecarry[:, a, half * P:(half + 1) * P], wp[:, a],
                                          start=(a == 0), stop=(a == 1))
            mm.then_inc(s_pj, 1)

        def windows(a, odd, lo):
            src = xv[:, a, odd:JW:2, lo:lo + 2 * LI + 1]
            return bass.AP(src.tensor, src.offset, [list(src.ap[0]), [1, 3], list(src.ap[1]), [2, LI]])

        def slices(xs, k, a, odd):
            n = LJ + 1 - odd
            return xs[:, k, a, :, odd * (LJ + 1) * LI:(odd * (LJ + 1) + n) * LI].rearrange("p i (r l) -> p i r l", l=LI)

        @block.scalar
        def _(act):
            act.wait_ge(s_w2, 16)
            nc.scalar.activation(wvh[:], wvt, ACT.Copy).then_inc(s_wh, 1)
            for b in range(B):
                act.wait_ge(s_st, STAT_STEPS * b + 6)
                nc.scalar.activation(gstd, gstd, ACT.Sqrt).then_inc(s_sta, 1)

            def v_out(g, u, q):
                t = STEPS * g + u
                cg, s = chunk_of(g, u)
                if q == 0 and s == 0:
                    wait(act, s_vs, cg + 1)
                if q % 2 == 0:
                    wait(act, s_vmm, 5 * t + q // 2 + 1)
                if q == 0:
                    wait(act, s_vg[(u + 1) % 2], 16 * Q * ((t + 1) // 2))
                bank = (5 * u + q // 2) % 2
                nc.scalar.activation(vtok[:, (Q * u + q) % VRING], psv[:, bank, q % 2], ACT.Copy,
                                     scale=vscale[:, s, q // 3:q // 3 + 1]).then_inc(s_vev, 1)

            def slice_hi(g, u):
                t = STEPS * g + u
                wait(act, s_xm, 2 * (t + 1))
                wait(act, s_vmm, 5 * (t - 1))
                for a in range(2):
                    for odd in range(2):
                        nc.scalar.activation(slices(xsh, u % 2, a, odd), windows(a, odd, 2 * LI * chunk_of(g, u)[1]),
                                             ACT.Copy).then_inc(s_xh, 1)

            def exp(g, u):
                t = STEPS * g + u
                wait(act, s_d3, t + 1)
                nc.scalar.activation(tl[:], tl[:], ACT.Exp, scale=SCALE).then_inc(s_exp, 1)

            def pool_out(g, u):
                t = STEPS * g + u
                cg, n = chunk_of(g, u)
                wait(act, s_um, t + 1)
                wait(act, s_l, STEPS * cg + (4 - STEPS if n < 4 else 0))
                if n == 0:
                    wait(act, s_ps, 2 * (cg + 1))
                for a in range(2):
                    last = nc.scalar.activation(
                        pooled[:, a, 4 * (n // 4):4 * (n // 4) + 4, 2 * (n % 4):2 * (n % 4) + 2],
                        psx[:, 0, a * P:(a + 1) * P].rearrange("p (l s i) -> p s l i", l=2, i=LI), ACT.Identity,
                        scale=pscale[:, a:a + 1], bias=pbias[:, a:a + 1])
                last.then_inc(s_pu, 1)

            act.wait_ge(s_stl, 16 * (2 * B + LJ * B))
            def v_outs(u, first, last):
                for q in range(first, last):
                    v_out(0, u, q)

            slice_hi(0, 0)
            pool_out(0, 0)
            slice_hi(0, 1)
            v_outs(0, 0, 4)
            pool_out(0, 1)
            v_outs(0, 4, Q)
            pool_out(0, 2)
            v_outs(1, 0, 4)
            pool_out(0, 3)
            exp(0, 0)
            v_outs(1, 4, Q)
            slice_hi(0, 2)
            pool_out(0, 4)
            pool_out(0, 5)
            exp(0, 1)

            def step(g, u):
                if present(g, u, 2):
                    if (u + 2) % STEPS == 0:
                        slice_hi(g, u + 2)
                    for q in range(Q):
                        v_out(g, u + 2, q)
                        if q == 3 and present(g, u, 3) and (u + 3) % STEPS:
                            slice_hi(g, u + 3)
                        if q == 7:
                            exp(g, u + 2)
                            if present(g, u, 6):
                                pool_out(g, u + 6)

            loop(act, step)

        @block.vector
        def _(dve):
            def image_stats(b):
                with dve.Fori(b * STAT_TILES // 2, (b + 1) * STAT_TILES // 2) as i:
                    for k in range(2):
                        dve.wait_ge(s_xt[k], 16 * (i + 1))
                        tile = xt[k].rearrange("p w (g c) -> p g w c", g=GROUPS)
                        for n in range(GROUPS):
                            last = nc.vector.bn_stats(
                                bn[:, n, bass.ds(2 * (i - b * STAT_TILES // 2) + k, 1)].rearrange("p a k -> p (a k)"),
                                tile[:, n])
                        last.then_inc(s_bn, 1)
                base = STAT_STEPS * b
                dve.wait_ge(s_bn, STAT_TILES * (b + 1))
                for n in range(GROUPS):
                    last = nc.vector.bn_aggr(mv[:, n], bn[:, n].rearrange("p t k -> p (t k)"))
                last.then_inc(s_bnag, 1)
                dve.wait_ge(s_bnag, b + 1)
                nc.vector.tensor_copy(mpart, mv[:, :, 0]).then_inc(s_st, 1)
                dve.wait_ge(s_stp, 2 * b + 1)
                nc.vector.tensor_copy(gmean[:, b], psx[:, 0, 0:GROUPS]).then_inc(s_st, 1)
                dve.wait_ge(s_st, base + 2)
                nc.vector.tensor_tensor(dev, mpart, gmean[:, b], ALU.subtract).then_inc(s_st, 1)
                dve.wait_ge(s_st, base + 3)
                nc.vector.tensor_tensor(dev, dev, dev, ALU.mult).then_inc(s_st, 1)
                dve.wait_ge(s_st, base + 4)
                nc.vector.tensor_tensor(vpart, dev, mv[:, :, 1], ALU.add).then_inc(s_st, 1)
                dve.wait_ge(s_stp, 2 * b + 2)
                nc.vector.tensor_scalar(gstd, psx[:, 0, 0:GROUPS], EPS, None, ALU.add).then_inc(s_st, 1)
                dve.wait_ge(s_sta, b + 1)
                nc.vector.reciprocal(gstd, gstd).then_inc(s_st, 1)
                dve.wait_ge(s_st, base + 7)
                for dst, src in ((mean_c, gmean[:, b]), (rstd_c, gstd)):
                    nc.vector.tensor_copy(dst[:, b, 1:C + 1].rearrange("p (g c) -> p g c", c=GC),
                                          src.unsqueeze(2).broadcast_to([P, GROUPS, GC])).then_inc(s_st, 1)
                dve.wait_ge(s_st, base + STAT_STEPS)

            dve.wait_ge(s_w2, 16)
            dve.wait_ge(s_wh, 1)
            nc.vector.tensor_tensor(wvl[:], wvt, wvh[:].bitcast(F32), ALU.subtract).then_inc(s_wl, 1)
            dve.wait_ge(s_zero, 2)
            for b in range(B):
                image_stats(b)
            nc.vector.memset(xv[:, :, 0], 0.0).then_inc(s_zero, 1)
            nc.vector.memset(xv[:, :, 1:JW, 0:1], 0.0).then_inc(s_zero, 1)
            nc.vector.memset(ag[:], 0.0).then_inc(s_c, 16)
            dve.wait_ge(s_zero, 4)
            dve.wait_ge(s_stl, 16 * (2 * B + LJ * B))
            nc.vector.tensor_tensor(nmean[:], cstat[:, :, 0], cstat[:, :, 1], ALU.mult).then_inc(s_st, 1)
            dve.wait_ge(s_st, STAT_DONE + 1)
            nc.vector.tensor_scalar(nmean[:], nmean[:], -1.0, None, ALU.mult).then_inc(s_st, 1)
            dve.wait_ge(s_w, W_DMAS * 16)

            by_q = tl[:].rearrange("p (q f) -> p q f", q=Q)
            by_f = tl[:].rearrange("p (q f) -> p f q", q=Q)

            def over_q(a):
                return a[:].unsqueeze(1).broadcast_to([P, Q, 3 * HK])

            def softmax_in(g, u):
                t = STEPS * g + u
                wait(dve, s_l, t + 1)
                wait(dve, s_as, 16 * t)
                nc.vector.tensor_tensor(tl[:].rearrange("p (a f) -> p a f", a=2), psl[:, :, 0:NA // 2],
                                        ab[:].rearrange("p (a f) -> p a f", a=2), ALU.add).then_inc(s_d1, 1)
                dve.wait_ge(s_d1, t + 1)
                nc.vector.tensor_reduce(tmax[:], by_f, AX.X, ALU.max).then_inc(s_d2, 1)
                dve.wait_ge(s_d2, t + 1)
                nc.vector.tensor_tensor(by_q, by_q, over_q(tmax), ALU.subtract).then_inc(s_d3, 1)

            def softmax_out(g, u):
                t = STEPS * g + u
                dve.wait_ge(s_exp, t + 1)
                nc.vector.tensor_reduce(tsum[:], by_f, AX.X, ALU.add).then_inc(s_d4, 1)
                dve.wait_ge(s_d4, t + 1)
                nc.vector.reciprocal(trec[:], tsum[:]).then_inc(s_d5, 1)
                dve.wait_ge(s_d5, t + 1)
                nc.vector.tensor_tensor(by_q, by_q, over_q(trec), ALU.mult).then_inc(s_p, 1)

            def y_out(g, u, h):
                t = STEPS * g + u
                cg, s = chunk_of(g, u)
                k = u % 2
                wait(dve, s_c, 16 * (t + 1) + 8 * (h + 1))
                if h == 0:
                    wait(dve, s_pj, 2 * (t - 1))
                    wait(dve, s_e2, t - 1)
                nc.vector.tensor_copy(yb[:, k, :, :, 16 * h:16 * h + 16],
                                      psy[:, :, JW:17 * JW].rearrange("p a (r j) -> p a j r", j=JW)).then_inc(s_ym, 1)
                if s == 0 and h == 0:
                    return
                row = yb[:, k, :, :, 15] if h else yb[:, (u + 1) % 2, :, :, ROWS - 1]
                dve.wait_ge(s_ym, 2 * t + h)
                nc.vector.tensor_tensor(row, psy[:, :, 0:JW], row, ALU.add).then_inc(s_ya, 1)

            def edges(g, u):
                t = STEPS * g + u
                cg, s = chunk_of(g, u)
                k = u % 2
                rows = slice(ROWS * s, ROWS * s + ROWS)
                wait(dve, s_ym, 2 * t + 2)
                wait(dve, s_ya, adds(g, u + 1, 0))
                wait(dve, s_e2, t)
                nc.vector.scalar_tensor_tensor(out=yb[:, k, :, 0], in0=yb[:, k, :, 0],
                                               scalar=inner[:, bass.ds(cg, 1)], in1=ecarry[:, :, rows],
                                               op0=ALU.mult, op1=ALU.add).then_inc(s_e1, 1)
                dve.wait_ge(s_e1, t + 1)
                nc.vector.tensor_copy(ecarry[:, :, rows], yb[:, k, :, JW - 1]).then_inc(s_e2, 1)

            def res_add(g, u, p):
                t = STEPS * g + u
                k = u % 2
                dve.wait_ge(s_rb, t + 1)
                dve.wait_ge(s_pj, 2 * t + p + 1)
                tiles = res[:, k, 2 * p:2 * p + 2]
                nc.vector.tensor_tensor(tiles, psp[:], tiles, ALU.add).then_inc(s_ra, 1)

            def less_mean(g, u):
                t = STEPS * g + u
                cg, s = chunk_of(g, u)
                if s == 0:
                    wait(dve, s_xv, 16 * XV_PIECES * (cg + 1))
                    if not (isinstance(g, int) and cg == 0):
                        wait(dve, s_row, cg)
                lo = 2 * LI * s + 1
                mean = gmean[:, bass.ds(cg // CPI, 1), lo // GC:lo // GC + 2 * LI // GC].rearrange("p o g -> p (o g)")
                mean = mean.unsqueeze(1).unsqueeze(3).broadcast_to([P, JW - 1, 2 * LI // GC, GC])
                for a in range(2):
                    cols = xv[:, a, 1:JW, lo:lo + 2 * LI].rearrange("p r (g c) -> p r g c", c=GC)
                    nc.vector.tensor_tensor(cols, cols, mean, ALU.subtract).then_inc(s_xm, 1)

            def pair(g, u):
                t = STEPS * g + u
                wait(dve, s_sl, 16 * (t + 1))
                nc.vector.tensor_tensor(slab[:, 0:4:2], slab[:, 0:4:2], slab[:, 1:4:2], ALU.add).then_inc(s_sp, 1)

            def slice_lo(g, u):
                t = STEPS * g + u
                for a in range(2):
                    for odd in range(2):
                        wait(dve, s_xh, 4 * t + 2 * a + odd + 1)
                        last = nc.vector.tensor_tensor(
                            slices(xsl, u % 2, a, odd), windows(a, odd, 2 * LI * chunk_of(g, u)[1]),
                            slices(xsh, u % 2, a, odd).bitcast(F32), ALU.subtract)
                last.then_inc(s_xs, 1)

            def next_row0(g, u):
                wait(dve, s_xs, STEPS * g + u + 1)
                m = inner[:, bass.ds(chunk_of(g, u)[0] + 1, 1)].unsqueeze(2).broadcast_to([P, 2, C + 1])
                nc.vector.tensor_tensor(xv[:, :, 0], xv[:, :, JW - 1], m, ALU.mult).then_inc(s_row, 1)

            def set_vscale(g, u):
                cg = chunk_of(g, u)[0]
                wait(dve, s_vev, Q * STEPS * cg)
                nc.vector.tensor_copy(vscale[:], rtok[:, bass.ds(cg // CPI, 1)].rearrange(
                    "p a s k -> p (a s) k")).then_inc(s_vs, 1)

            def set_pscale(g, u):
                cg = chunk_of(g, u)[0]
                wait(dve, s_pu, STEPS * cg)
                where = bass.ds(cg // CPI, 1)
                nc.vector.tensor_copy(pscale[:], cstat[:, where, 1].rearrange("p a k -> p (a k)")).then_inc(s_ps, 1)
                nc.vector.tensor_copy(pbias[:], nmean[:, where].rearrange("p a k -> p (a k)")).then_inc(s_ps, 1)

            dve.wait_ge(s_st, STAT_DONE + 2)
            set_vscale(0, 0)
            set_pscale(0, 0)
            less_mean(0, 0)
            pair(0, 0)
            slice_lo(0, 0)
            less_mean(0, 1)
            pair(0, 1)
            slice_lo(0, 1)
            pair(0, 2)
            less_mean(0, 2)
            pair(0, 3)
            softmax_in(0, 0)
            softmax_out(0, 0)
            pair(0, 4)
            slice_lo(0, 2)
            pair(0, 5)
            softmax_in(0, 1)

            def step(g, u):
                ahead, here, behind = present(g, u, 1), present(g, u, 0), present(g, u, -1)
                if u == STEPS - 2 and present(g, u, 2):
                    set_vscale(g, u + 2)
                if ahead:
                    softmax_out(g, u + 1)
                if here:
                    y_out(g, u, 0)
                if behind:
                    edges(g, u - 1)
                if present(g, u, 2) and (u + 2) % STEPS == 0:
                    less_mean(g, u + 2)
                    slice_lo(g, u + 2)
                if here:
                    y_out(g, u, 1)
                if u == 2 and present(g, u, 6):
                    set_pscale(g, u + 6)
                if behind and u == STEPS - 2:
                    res_add(g, u - 1, 0)
                more = present(g, u, 3) and (u + 3) % STEPS
                if more:
                    less_mean(g, u + 3)
                if behind and u != STEPS - 2:
                    res_add(g, u - 1, 0)
                if present(g, u, 2) and u == STEPS - 2:
                    softmax_in(g, u + 2)
                    if present(g, u, 6):
                        pair(g, u + 6)
                if more:
                    slice_lo(g, u + 3)
                if u == 4 and present(g, u, 4):
                    next_row0(g, u + 3)
                if u != STEPS - 2:
                    if present(g, u, 6):
                        pair(g, u + 6)
                    if present(g, u, 2):
                        softmax_in(g, u + 2)
                if behind:
                    res_add(g, u - 1, 1)

            loop(dve, step)
            dve.wait_ge(s_rb, NT + 1)
            dve.wait_ge(s_pj, 2 * NT + 1)
            nc.vector.tensor_tensor(res[:, 0, 0:2], psp[:], res[:, 0, 0:2], ALU.add).then_inc(s_ra, 1)


STAT_STEPS = 9
STAT_DONE = STAT_STEPS * B


def kernel(**inputs):
    import numpy as np
    import concourse.bacc as bacc
    from concourse.bass_utils import run_bass_kernel_spmd

    conv_wt = np.asarray(inputs["L0_conv_conv_w"]).reshape(Q, C, C).transpose(2, 0, 1)
    attn_wt = np.asarray(inputs["L0_conv_attn_w"]).reshape(HEADS, 3, 3, Q, C).transpose(4, 3, 2, 0, 1).reshape(C, NA)
    attn_b = np.asarray(inputs["L0_conv_attn_b"]).reshape(HEADS, 3, 3, Q).transpose(3, 2, 0, 1).reshape(NA)
    h = np.arange(P)
    arrays = {
        "x": np.asarray(inputs["x"]), "conv_wt": conv_wt, "attn_wt": attn_wt, "attn_b": attn_b,
        "proj_wt": np.asarray(inputs["L0_conv_proj_w"]).T, "proj_b": np.asarray(inputs["L0_conv_proj_b"]),
        "pool_m": np.where(h[:, None] // 2 == np.arange(64)[None], 0.25, 0.0).astype(np.float32),
        "avg_m": np.full((P, P), 1.0 / P, np.float32),
        "inner_m": np.where(np.arange(CHUNKS) % CPI == 0, 0.0, 1.0).astype(np.float32)[None].repeat(P, 0),
    }
    arrays = {f"in_{k}": np.ascontiguousarray(v) for k, v in arrays.items()}
    nc = bacc.Bacc("TRN2", target_bir_lowering=False, num_devices=1)
    args = [nc.dram_tensor(k, v.shape, F32, kind="ExternalInput").ap() for k, v in arrays.items()]
    out = nc.dram_tensor("out_y", (B, H, W, C), F32, kind="ExternalOutput").ap()
    build(nc, *args, out)
    r = run_bass_kernel_spmd(nc, [arrays], core_ids=[0])
    return r.results[0]["out_y"]
```
